# Optimizing a Trainium2 kernel written in Bass

```python
import numpy as np
import jax
import jax.numpy as jnp

def _softmax(x, axis=-1):
    return jax.nn.softmax(x, axis=axis)

def _gelu(x):
    return jax.nn.gelu(x, approximate=True)

def _silu(x):
    return jax.nn.silu(x)

def _sigmoid(x):
    return jax.nn.sigmoid(x)

def _layernorm(x, axis=-1, eps=1e-05):
    m = jnp.mean(x, axis=axis, keepdims=True)
    v = jnp.var(x, axis=axis, keepdims=True)
    return (x - m) / jnp.sqrt(v + eps)

def _scatter_add(tgt, idx, src, axis=0):
    return tgt.at[idx].add(src)

def _segment_sum(src, seg, n):
    return jax.ops.segment_sum(src, seg, n)
kernel_name = 'mk_gnn_preln_d1_gnn_r8_89997f'

def setup_inputs(seed: int=0):
    np.random.seed(seed)
    _w = jnp.asarray

    def _rec_inputs():
        import jax
        import jax.numpy as jnp
        _gk = jax.random.key(seed)
        x = -0.0009044 + 1 * jax.random.normal(jax.random.fold_in(_gk, 1), (12500, 32), jnp.float32)
        _s = jax.random.randint(jax.random.fold_in(_gk, 2), (200000,), 0, 12500, jnp.int32)
        _d = jax.random.randint(jax.random.fold_in(_gk, 3), (200000,), 0, 12500, jnp.int32)
        _loop = jnp.arange(12500, dtype=jnp.int32)
        src = jnp.concatenate([_s, _d, _loop])
        dst = jnp.concatenate([_d, _s, _loop])
        _o = jnp.argsort(dst, stable=True)
        src = src[_o]
        dst = dst[_o]
        edge_attr_32 = 0.000196303 + 1.00016 * jax.random.normal(jax.random.fold_in(_gk, 11), (412500, 32), jnp.float32)
        return (x, src, dst, edge_attr_32)
    x, src, dst, edge_attr_32 = _rec_inputs()

    def _L0_gnn_setup():
        import jax, jax.numpy as jnp
        import numpy as np
        N_NODES = 6250
        N_EDGES = 100000
        X_DIM = 32
        E_DIM = 32
        HID = 64
        OUT = 32
        key = jax.random.key(seed)
        ks = jax.random.split(key, 6)
        x = jax.random.normal(ks[0], (N_NODES, X_DIM), dtype=jnp.float32)
        edge_index = jax.random.randint(ks[1], (2, N_EDGES), 0, N_NODES, dtype=jnp.int64)
        edge_attr = jax.random.normal(ks[2], (N_EDGES, E_DIM), dtype=jnp.float32)
        in_dim = 2 * X_DIM + E_DIM
        W1 = jax.random.normal(ks[3], (in_dim, HID), dtype=jnp.float32) * (1.0 / np.sqrt(in_dim))
        b1 = jnp.zeros((HID,), dtype=jnp.float32)
        W2 = jax.random.normal(ks[4], (HID, OUT), dtype=jnp.float32) * (1.0 / np.sqrt(HID))
        b2 = jnp.zeros((OUT,), dtype=jnp.float32)
        return {'x': x, 'edge_index': edge_index, 'edge_attr': edge_attr, 'W1': W1, 'b1': b1, 'W2': W2, 'b2': b2}
    _L0_gnn_all = _L0_gnn_setup()
    _L0_gnn_in = {k: v for k, v in _L0_gnn_all.items() if k in ('W1', 'b1', 'W2', 'b2')}
    del _L0_gnn_all
    return {'x': x, 'src': src, 'dst': dst, 'edge_attr_32': edge_attr_32, 'L0_gnn_W1': _L0_gnn_in['W1'], 'L0_gnn_b1': _L0_gnn_in['b1'], 'L0_gnn_W2': _L0_gnn_in['W2'], 'L0_gnn_b2': _L0_gnn_in['b2']}

def reference(x, src, dst, edge_attr_32, L0_gnn_W1, L0_gnn_b1, L0_gnn_W2, L0_gnn_b2):
    import jax
    import jax.numpy as jnp

    def _L0_gnn_ref(x, edge_index, edge_attr, W1, b1, W2, b2):
        import jax, jax.numpy as jnp
        import numpy as np
        N_NODES = 6250
        N_EDGES = 100000
        X_DIM = 32
        E_DIM = 32
        HID = 64
        OUT = 32
        num_nodes = x.shape[0]
        rol, col = (edge_index[0], edge_index[1])
        e_feat = jnp.concatenate([x[rol], x[col], edge_attr], axis=-1)
        h = jax.nn.relu(e_feat @ W1 + b1)
        v = h @ W2 + b2
        x_cand = jax.ops.segment_max(v, col, num_segments=num_nodes)
        return jnp.maximum(x_cand, x[:, -v.shape[-1]:])
    edge_index = jnp.stack([src, dst])
    h = jnp.maximum(_layernorm(x, axis=-1), 0.0)
    x = x + _L0_gnn_ref(h, edge_index, edge_attr_32, L0_gnn_W1, L0_gnn_b1, L0_gnn_W2, L0_gnn_b2)
    return x

_drawn_inputs = setup_inputs


def setup_inputs(seed=0):
    import zlib

    import numpy as np

    out = dict(_drawn_inputs(seed))
    spreads = {'L0_gnn_b1': (0.0, 0.1), 'L0_gnn_b2': (0.0, 0.1)}
    factors = {}
    for name, (base, spread) in spreads.items():
        noise = np.random.default_rng([zlib.crc32(name.encode()), seed]).standard_normal(out[name].shape)
        drawn = base * np.exp(spread * noise) if base else spread * noise
        out[name] = jnp.asarray(drawn.astype(out[name].dtype))
    for name, factor in factors.items():
        out[name] = (out[name] * factor).astype(out[name].dtype)
    return out
```

```python
from contextlib import ExitStack

import concourse.bass as bass
from concourse import mybir

F32 = mybir.dt.float32
BF16 = mybir.dt.bfloat16
I32 = mybir.dt.int32
U32 = mybir.dt.uint32
ALU = mybir.AluOpType
ACT = mybir.ActivationFunctionType
AX = mybir.AxisListType

P = 128
J = 4
CE = P * J
RING = 4
EPS = 1e-5


def gnn_layer(nc, x, src, dst, edge_attr, W1, b1, W2, b2, out):
    N, D = x.shape
    E = src.shape[0]
    HID = W1.shape[1]
    C = -(-E // CE)
    LAST = E - CE
    T = -(-N // P)
    NW = 2 * T
    TAIL = N - (T - 1) * P
    TG = -(-(T + 1) // J)
    B = -(-C // P)
    assert D == 32 and HID == 64 and W2.shape[1] == D and C > 2 and (C - 2) % RING == 0
    FULLP = N // T
    REST = N - FULLP * T
    assert FULLP < P

    h_dram = nc.dram_tensor("h_rows", (N, D), F32, kind="Internal").ap()

    def chunks_of(b):
        return min(P, C - b * P)

    ctx = ExitStack()
    with ctx:
        def sb(name, shape, dt=F32):
            return ctx.enter_context(nc.sbuf_tensor(name, shape, dt))

        def pb(name, shape, dt=F32):
            return ctx.enter_context(nc.psum_tensor(name, shape, dt))

        def sem(name):
            return ctx.enter_context(nc.semaphore(name))

        node_term = sb("node_term", [P, 2 * J * TG, HID])
        best = sb("best", [P, NW, D])
        h_win = sb("h_win", [P, J * TG, D])
        x_even = sb("x_even", [P, T, D])
        dst_rows = sb("dst_rows", [P, B, CE], I32)
        src_cols = sb("src_cols", [P, J * (C + RING)], I32)
        loc_cols = sb("loc_cols", [P, J * (C + 1)])
        end_cols = sb("end_cols", [P, J * C])
        keep_cols = sb("keep_cols", [P, J * (C + 1)], BF16)
        firsts = sb("firsts", [1, C + 1], I32)
        best_at = sb("best_at", [1, C + 1], I32)
        term_at = sb("term_at", [1, C + 1], I32)
        ident = sb("ident", [P, P])
        ident_bf = sb("ident_bf", [P, P], BF16)
        iota_n = sb("iota_n", [P, P])
        iota_i = sb("iota_i", [P, P], I32)
        w1_pair = sb("w1_pair", [P, P])
        w1_dst = sb("w1_dst", [P, J, HID])
        w2_pair = sb("w2_pair", [P, 2 * D])
        b1_col = sb("b1_col", [P, 1])
        b2_col = sb("b2_col", [P, 1])
        idx_ring = sb("idx_ring", [P, RING, J], I32)
        feat = sb("feat", [P, RING, 2, 2, 2 * D])
        onehot = sb("onehot", [P, 2, J, P])
        onehot_t = sb("onehot_t", [P, J, P])
        keep_wide = sb("keep_wide", [P, P], BF16)
        term = sb("term", [P, HID])
        feat_t = sb("feat_t", [P, 2, P])
        hidden = sb("hidden", [P, 2, P])
        value = sb("value", [P, P])
        running = sb("running", [P, P])
        ends = sb("ends", [P, J, D])
        picked4 = sb("picked4", [P, D])
        mean = sb("mean", [P, T])
        var = sb("var", [P, T])
        rstd = sb("rstd", [P, T])
        base_i = sb("base_i", [P, B], I32)
        base_f = sb("base_f", [P, B])
        prep = sb("prep", [P, 2, 4, CE])
        dst_f = sb("dst_f", [P, 2, CE])
        turned_h = sb("turned_h", [P, P])

        flat_term = node_term[:].rearrange("p w k -> p (w k)")
        cent = flat_term[:, 0:T * D].rearrange("p (t d) -> p t d", d=D)
        sq = flat_term[:, T * D:2 * T * D].rearrange("p (t d) -> p t d", d=D)
        h_even = sq
        src_rows = flat_term[:, 2 * T * D:2 * T * D + B * CE].bitcast(I32).rearrange("p (b e) -> p b e", e=CE)
        assert 2 * T * D + B * CE <= 2 * J * TG * HID

        ps_feat = pb("ps_feat", [P, 2, P])
        ps_onehot = pb("ps_onehot", [P, J, P])
        ps_hidden = pb("ps_hidden", [P, 2, 2 * P])
        ps_value = pb("ps_value", [P, 4 * P])
        ps_keep = pb("ps_keep", [P, 4 * P])
        ps_ends = pb("ps_ends", [P, 4 * P])
        ps_pick = pb("ps_pick", [P, 4 * P])

        s_names = """const_ready row_pad best_zero shift_pad pads base_step x_in x_pad w_in w_zero src_in dst_in firsts_in at_ready
            cent_done sq_done var_ready std_ready norm_step h_even_done h_stored h_win_in
            cast_done arrays_done prep_turned prep_out ht_turned ht_out term_made term_out odd_in
            chunk_open chunk_begun feat_turned feat_t_ready onehot_ready onehot_turned onehot_t_ready
            term_ready wide_ready keep_ready hid_sum hid_ready val_sum val_ready run_ready ends_turned
            ends_ready pick_ready picked_max best_done odd_out x_win_in final_step out_ready
            out_done""".split()
        S = {n: sem(n) for n in s_names}
        s_gather = [sem(f"gathered{r}") for r in range(RING)]
        s_attr = [sem(f"attr_in{r}") for r in range(RING)]

        flat_best = best[:].rearrange("p w d -> p (w d)")
        shifted = flat_term[:, 0:T * D].rearrange("p (t d) -> p t d", d=D)

        def steps(eng, step, first=0, beyond=0):
            for s in range(2):
                step(s, s % RING, s // RING)
            with eng.Fori(0, (C - 2) // RING) as i:
                for u in range(RING):
                    step(i * RING + (2 + u), (2 + u) % RING, i + (2 + u) // RING)

        def known(s):
            return isinstance(s, int)

        PIECES = [(0, FULLP // 16 * 16), (FULLP // 16 * 16, FULLP)]

        def even_dmas(dma, dram, tile, to_dram, done):
            for a, z in PIECES:
                if z > a:
                    d = dram[a * T:z * T, :].rearrange("(p t) d -> p t d", t=T)
                    s_ = tile[a:z, :, :]
                    (dma(d, s_) if to_dram else dma(s_, d)).then_inc(done, 16)
            d = dram[FULLP * T:N, :].rearrange("(p t) d -> p t d", p=1)
            s_ = tile[FULLP:FULLP + 1, 0:REST, :]
            (dma(d, s_) if to_dram else dma(s_, d)).then_inc(done, 16)

        EVEN = 16 * (1 + sum(z > a for a, z in PIECES))

        def win_dmas(dma, dram, tile, to_dram, done):
            d = dram[0:(T - 1) * P, :].rearrange("(t p) d -> p t d", p=P)
            s_ = tile[:, 0:T - 1, :]
            (dma(d, s_) if to_dram else dma(s_, d)).then_inc(done, 16)
            d = dram[(T - 1) * P:N, :]
            s_ = tile[0:TAIL, T - 1, :]
            (dma(d, s_) if to_dram else dma(s_, d)).then_inc(done, 16)

        def row_dmas(dma, vec, tile, done):
            for b in range(B):
                whole = min(P, C - 1 - b * P)
                dma(tile[0:whole, b, :],
                    vec[b * P * CE:(b * P + whole) * CE].rearrange("(q e) -> q e", e=CE)).then_inc(done, 16)
                if b == B - 1:
                    dma(tile[whole:whole + 1, b, :],
                        vec[LAST:E].rearrange("(q e) -> q e", q=1)).then_inc(done, 16)

        NROW = B + 1
        attr = edge_attr.rearrange("e f -> (e f)")
        NBD = 4 + 2 + J + 2 + J

        best_even = x_even
        block = ctx.enter_context(nc.Block())

        @block.sync
        def _(sp):
            sp.wait_ge(S["x_pad"], 1)
            even_dmas(sp.dma_start, x, x_even, False, S["x_in"])
            row_dmas(sp.dma_start, src, src_rows, S["src_in"])
            sp.wait_ge(S["row_pad"], 2)
            row_dmas(sp.dma_start, dst, dst_rows, S["dst_in"])
            sp.dma_start(firsts[:, 0:C - 1],
                         dst[0:(C - 1) * CE].rearrange("(a c e) -> a c e", a=1, e=CE)[:, :, 0],
                         allow_slow_non_contiguous=True).then_inc(S["firsts_in"], 16)
            sp.dma_start(firsts[:, C - 1:C],
                         dst[LAST:LAST + 1].rearrange("(a c) -> a c", a=1)).then_inc(S["firsts_in"], 16)
            sp.wait_ge(S["w_zero"], 3)
            for z, row in enumerate((0, 2 * D)):
                for a in range(2):
                    k = 2 * D * z + D * a
                    sp.dma_start(w1_pair[k:k + D, HID * a:HID * a + HID], W1[row:row + D, :]).then_inc(S["w_in"], 16)
            for t in range(J):
                sp.dma_start(w1_dst[D * t:D * t + D, t, :], W1[D:2 * D, :]).then_inc(S["w_in"], 16)
                sp.dma_start(b2_col[D * t:D * t + D, :], b2.rearrange("(p a) -> p a", a=1)).then_inc(S["w_in"], 16)
            for a in range(2):
                sp.dma_start(w2_pair[HID * a:HID * a + HID, D * a:D * a + D], W2).then_inc(S["w_in"], 16)
                sp.dma_start(b1_col[HID * a:HID * a + HID, :], b1.rearrange("(p a) -> p a", a=1)).then_inc(S["w_in"], 16)
            sp.wait_ge(S["h_even_done"], 2)
            even_dmas(sp.dma_start, h_dram, h_even, True, S["h_stored"])
            sp.wait_ge(S["h_stored"], EVEN)
            sp.wait_ge(S["pads"], 4)
            win_dmas(sp.dma_start, h_dram, h_win, False, S["h_win_in"])
            sp.wait_ge(S["term_out"], TG)
            half = P // 2
            ev = node_term[:].rearrange("p (t o) k -> p t o k", o=2)
            sp.dma_start(ev[0:half, 0:T, 1, :], ev[half:P, 0:T, 0, :]).then_inc(S["odd_in"], 16)
            sp.dma_start(ev[half:P, 0:T, 1, :], ev[0:half, 1:T + 1, 0, :]).then_inc(S["odd_in"], 16)

            def step(s, slot, turn):
                sp.wait_ge(S["chunk_open"], s + 1)
                sp.dma_start(feat[:, slot, :, 1, :],
                             attr[bass.ds(s * (CE * D), CE * D)].rearrange("(p c k) -> p c k", p=P, c=2)
                             ).then_inc(s_attr[slot], 16)

            for s in range(2):
                step(s, s % RING, 0)
            with sp.Fori(0, (C - 2) // RING - 1) as i:
                for u in range(RING):
                    step(i * RING + (2 + u), (2 + u) % RING, 0)
            for s in range(C - RING, C - 1):
                step(s, s % RING, 0)
            sp.wait_ge(S["chunk_open"], C)
            sp.dma_start(feat[:, (C - 1) % RING, :, 1, :],
                         attr[LAST * D:E * D].rearrange("(p c k) -> p c k", p=P, c=2)).then_inc(s_attr[(C - 1) % RING], 16)

            win_dmas(sp.dma_start, x, x_even, False, S["x_win_in"])
            sp.wait_ge(S["best_done"], C)
            bv = best[:].rearrange("p (t o) d -> p t o d", o=2)
            sp.dma_start(shifted[half:P, 0:T, :], bv[0:half, 0:T, 1, :]).then_inc(S["odd_out"], 16)
            sp.dma_start(shifted[0:half, 1:T, :], bv[half:P, 0:T - 1, 1, :]).then_inc(S["odd_out"], 16)
            sp.wait_ge(S["out_ready"], 1)
            win_dmas(sp.dma_start, out, best_even, True, S["out_done"])
            sp.wait_ge(S["out_done"], 32)

        @block.gpsimd
        def _(pool):
            nc.gpsimd.memset(ident[:], 0.0).then_inc(S["const_ready"], 1)
            pool.wait_ge(S["const_ready"], 1)
            nc.gpsimd.affine_select(out=ident[:], in_=ident[:], compare_op=ALU.not_equal, fill=1.0, base=0,
                                    pattern=[[-1, P]], channel_multiplier=1).then_inc(S["const_ready"], 1)
            nc.gpsimd.iota(iota_i[:], pattern=[[1, P]], base=0, channel_multiplier=0).then_inc(S["const_ready"], 1)
            nc.gpsimd.memset(best[:], 0.0).then_inc(S["best_zero"], 1)
            pool.wait_ge(S["h_stored"], EVEN)

            def step(s, slot, turn):
                pool.wait_ge(S["chunk_open"], s + 1)
                pool.sem_inc(S["chunk_begun"], 1)
                for j in range(J):
                    nc.gpsimd.indirect_dma_start(
                        feat[:, slot, j // 2, 0, D * (j % 2):D * (j % 2) + D], None, h_dram,
                        bass.IndirectOffsetOnAxis(ap=idx_ring[:, slot, j:j + 1].bitcast(U32), axis=0),
                    ).then_inc(s_gather[slot], 16)

            steps(pool, step)

        @block.tensor
        def _(pe):
            pe.wait_ge(S["const_ready"], 5)
            ps2 = (ps_ends, ps_pick)
            k = 0
            for b in range(B):
                q = chunks_of(b)
                for a in range(4):
                    if a == 0:
                        pe.wait_ge(S["cast_done"], 2 * b + 1)
                    if a == 1:
                        pe.wait_ge(S["arrays_done"], b + 1)
                    if k >= 2:
                        pe.wait_ge(S["prep_out"], k - 1)
                    for j in range(J):
                        mm = pe.transpose(ps2[k % 2][:, P * j:P * j + q], prep[0:q, b % 2, a, j:CE:J], ident[0:q, 0:q])
                    mm.then_inc(S["prep_turned"], 1)
                    k += 1
            pe.wait_ge(S["h_win_in"], 32)
            pe.wait_ge(S["w_in"], 16 * NBD)
            for g in range(TG):
                if g >= 1:
                    pe.wait_ge(S["ht_out"], g)
                pe.transpose(ps_value[:, 0:P], h_win[:, J * g:J * g + J, :].rearrange("p t d -> p (t d)"),
                             ident[:]).then_inc(S["ht_turned"], 1)
                pe.wait_ge(S["ht_out"], g + 1)
                if g >= 1:
                    pe.wait_ge(S["term_out"], g)
                pe.matmul(ps_keep[:, 0:J * HID], turned_h[:], w1_dst[:].rearrange("p t k -> p (t k)"),
                          start=True, stop=True).then_inc(S["term_made"], 1)

            def pick(s, par):
                pe.wait_ge(S["ends_ready"], s + 1)
                for j in range(J):
                    mm = pe.matmul(ps_pick[:, D * j:D * j + D], onehot[:, par, j, :], ends[:, j, :],
                                   start=(j == 0), stop=(j == J - 1), skip_group_check=True)
                mm.then_inc(S["pick_ready"], 1)

            def turn_best(s):
                pe.wait_ge(S["run_ready"], s + 1)
                pe.transpose(ps_ends[:, 0:P], running[:], ident[:]).then_inc(S["ends_turned"], 1)

            def step(s, slot, turn):
                pe.wait_ge(s_gather[slot], (turn + 1) * (16 * J))
                pe.wait_ge(s_attr[slot], (turn + 1) * 16)
                for c in range(2):
                    mm = pe.transpose(ps_feat[:, c, :], feat[:, slot, c, :, :].rearrange("p z k -> p (z k)"), ident[:])
                mm.then_inc(S["feat_turned"], 1)
                pe.wait_ge(S["onehot_ready"], s + 1)
                for j in range(J):
                    mm = pe.transpose(ps_onehot[:, j, :], onehot[:, slot % 2, j, :], ident[:])
                mm.then_inc(S["onehot_turned"], 1)
                if not (known(s) and s == 0):
                    turn_best(s - 1)
                pe.wait_ge(S["wide_ready"], s + 1)
                pe.matmul(ps_keep[:, 0:P], keep_wide[:], ident_bf[:], start=True,
                          stop=True).then_inc(S["keep_ready"], 1)
                pe.wait_ge(S["feat_t_ready"], s + 1)
                for c in range(2):
                    pe.matmul(ps_hidden[:, 0, P * c:P * c + P], w1_pair[:], feat_t[:, c, :],
                              start=(c == 0), stop=False, skip_group_check=True)
                pe.wait_ge(S["term_ready"], s + 1)
                pe.wait_ge(S["onehot_t_ready"], s + 1)
                for a in range(2):
                    mm = pe.matmul(ps_hidden[HID * a:HID * a + HID, 0, :], term[:], onehot_t[:, a:J:2, :],
                                   start=False, stop=True, skip_group_check=True)
                mm.then_inc(S["hid_sum"], 1)
                if not (known(s) and s == 0):
                    pick(s - 1, (slot + 1) % 2)
                pe.wait_ge(S["hid_ready"], s + 1)
                for c in range(2):
                    mm = pe.matmul(ps_value[HID * c:HID * c + HID, 0:P], w2_pair[:], hidden[:, c, :],
                                   start=True, stop=True, skip_group_check=True)
                mm.then_inc(S["val_sum"], 1)

            pe.wait_ge(S["prep_out"], 4 * B)
            steps(pe, step)
            turn_best(C - 1)
            pick(C - 1, (C - 1) % 2)

        @block.scalar
        def _(act):
            halves = [(0, T // 2), (T // 2, T)]
            for n, (a, z) in enumerate(halves):
                act.wait_ge(S["cent_done"], n + 1)
                nc.scalar.activation(sq[:, a:z, :], cent[:, a:z, :], ACT.Square).then_inc(S["sq_done"], 1)
            act.wait_ge(S["var_ready"], 1)
            nc.scalar.activation(mean[:], var[:], ACT.Sqrt).then_inc(S["std_ready"], 1)

            def casts(b):
                act.wait_ge(S["src_in"], 16 * NROW)
                act.wait_ge(S["dst_in"], 16 * NROW)
                q = chunks_of(b)
                if b >= 2:
                    act.wait_ge(S["prep_turned"], 4 * (b - 1))
                    act.wait_ge(S["arrays_done"], b - 1)
                nc.scalar.copy(prep[0:q, b % 2, 0, :], src_rows[0:q, b, :]).then_inc(S["cast_done"], 1)
                nc.scalar.copy(dst_f[0:q, b % 2, :], dst_rows[0:q, b, :]).then_inc(S["cast_done"], 1)

            ps2 = (ps_ends, ps_pick)
            k = 0
            casts(0)
            for b in range(B):
                q = chunks_of(b)
                if b + 1 < B:
                    casts(b + 1)
                for a, table in enumerate((src_cols, loc_cols, keep_cols, end_cols)):
                    act.wait_ge(S["prep_turned"], k + 1)
                    to = table[:, J * P * b:J * P * b + J * q].rearrange("p (q j) -> p j q", j=J)
                    nc.scalar.copy(to, ps2[k % 2][:].rearrange("p (j q) -> p j q", j=J)[:, :, 0:q]).then_inc(S["prep_out"], 1)
                    k += 1
            for g in range(TG):
                act.wait_ge(S["ht_turned"], g + 1)
                nc.scalar.copy(turned_h[:], ps_value[:, 0:P]).then_inc(S["ht_out"], 1)
                act.wait_ge(S["term_made"], g + 1)
                nc.scalar.copy(node_term[:, 2 * J * g:2 * J * g + 2 * J:2, :],
                               ps_keep[:, 0:J * HID].rearrange("p (t k) -> p t k", t=J)).then_inc(S["term_out"], 1)
            act.wait_ge(S["odd_in"], 32)
            act.wait_ge(S["at_ready"], 2)

            def step(s, slot, turn):
                at = act.value_load(term_at[0:1, bass.ds(s, 1)], min_val=0, max_val=(NW - 1) * HID)
                nc.scalar.copy(term[:], flat_term[:, bass.ds(at, HID)]).then_inc(S["term_ready"], 1)
                act.wait_ge(S["feat_turned"], s + 1)
                nc.scalar.copy(feat_t[:], ps_feat[:]).then_inc(S["feat_t_ready"], 1)
                act.wait_ge(S["onehot_turned"], s + 1)
                nc.scalar.copy(onehot_t[:], ps_onehot[:]).then_inc(S["onehot_t_ready"], 1)
                act.wait_ge(S["hid_sum"], s + 1)
                nc.scalar.activation(hidden[:], ps_hidden[:, 0, :].rearrange("p (c q) -> p c q", c=2), ACT.Relu,
                                     bias=b1_col[:, 0:1]).then_inc(S["hid_ready"], 1)
                act.wait_ge(S["val_sum"], s + 1)
                nc.scalar.activation(value[:], ps_value[:, 0:P], ACT.Identity,
                                     bias=b2_col[:, 0:1]).then_inc(S["val_ready"], 1)

            act.wait_ge(S["w_in"], 16 * NBD)
            steps(act, step)

        @block.vector
        def _(dve):
            nc.vector.memset(x_even[96:P, :, :], 0.0).then_inc(S["x_pad"], 1)
            nc.vector.memset(w1_pair[:], 0.0).then_inc(S["w_zero"], 1)
            nc.vector.memset(w1_dst[:], 0.0).then_inc(S["w_zero"], 1)
            nc.vector.memset(w2_pair[:], 0.0).then_inc(S["w_zero"], 1)
            nc.vector.memset(h_win[:, T - 1:J * TG, :], 0.0).then_inc(S["pads"], 1)
            nc.vector.memset(src_cols[:, J * C:J * (C + RING)], 0).then_inc(S["pads"], 1)
            nc.vector.memset(loc_cols[:, J * C:J * (C + 1)], 0.0).then_inc(S["pads"], 1)
            nc.vector.memset(keep_cols[:, J * C:J * (C + 1)], 0.0).then_inc(S["pads"], 1)
            nc.vector.memset(dst_rows[:, B - 1, :], 0).then_inc(S["row_pad"], 1)
            nc.vector.memset(firsts[:, C:C + 1], 0).then_inc(S["row_pad"], 1)
            dve.wait_ge(S["x_in"], EVEN)
            halves = [(0, T // 2), (T // 2, T)]
            n = 0
            for a, z in halves:
                nc.vector.reduce_sum(mean[:, a:z], x_even[:, a:z, :], AX.X).then_inc(S["norm_step"], 1)
                dve.wait_ge(S["norm_step"], n + 1)
                nc.vector.tensor_scalar(mean[:, a:z], mean[:, a:z], 1.0 / D, None, ALU.mult).then_inc(S["norm_step"], 1)
                dve.wait_ge(S["norm_step"], n + 2)
                nc.vector.tensor_tensor(cent[:, a:z, :], x_even[:, a:z, :],
                                        mean[:, a:z].unsqueeze(2).broadcast_to([P, z - a, D]),
                                        ALU.subtract).then_inc(S["cent_done"], 1)
                n += 2
            for i, (a, z) in enumerate(halves):
                dve.wait_ge(S["sq_done"], i + 1)
                nc.vector.reduce_sum(var[:, a:z], sq[:, a:z, :], AX.X).then_inc(S["norm_step"], 1)
                n += 1
            dve.wait_ge(S["norm_step"], n)
            nc.vector.tensor_scalar(var[:], var[:], 1.0 / D, EPS, ALU.mult, ALU.add).then_inc(S["var_ready"], 1)
            dve.wait_ge(S["const_ready"], 3)
            nc.vector.tensor_copy(ident_bf[:], ident[:]).then_inc(S["const_ready"], 1)
            nc.vector.tensor_copy(iota_n[:], iota_i[:]).then_inc(S["const_ready"], 1)
            dve.wait_ge(S["std_ready"], 1)
            nc.vector.reciprocal(rstd[:], mean[:]).then_inc(S["norm_step"], 1)
            dve.wait_ge(S["norm_step"], n + 1)
            for a, z in halves:
                nc.vector.scalar_tensor_tensor(out=h_even[:, a:z, :], in0=cent[:, a:z, :], scalar=0.0,
                                               in1=rstd[:, a:z].unsqueeze(2).broadcast_to([P, z - a, D]),
                                               op0=ALU.max, op1=ALU.mult).then_inc(S["h_even_done"], 1)
            dve.wait_ge(S["firsts_in"], 32)
            for table, width in ((best_at, D), (term_at, HID)):
                nc.vector.tensor_scalar(table[:], firsts[:], 6, width.bit_length() - 1, ALU.logical_shift_right,
                                        ALU.logical_shift_left).then_inc(S["at_ready"], 1)
            dve.wait_ge(S["dst_in"], 16 * NROW)
            nc.vector.tensor_scalar(base_i[:], dst_rows[:, :, 0], 6, 6, ALU.logical_shift_right,
                                    ALU.logical_shift_left).then_inc(S["base_step"], 1)
            dve.wait_ge(S["base_step"], 1)
            nc.vector.tensor_copy(base_f[:], base_i[:]).then_inc(S["base_step"], 1)
            dve.wait_ge(S["base_step"], 2)
            for b in range(B):
                q = chunks_of(b)
                dve.wait_ge(S["cast_done"], 2 * b + 2)
                if b >= 2:
                    dve.wait_ge(S["prep_turned"], 4 * (b - 1))
                d = dst_f[0:q, b % 2, :]
                _, loc, keep, end = (prep[0:q, b % 2, a, :] for a in range(4))
                nc.vector.tensor_scalar(loc, d, base_f[0:q, b:b + 1], None, ALU.subtract)
                nc.vector.memset(keep[:, 0:J], 0.0)
                nc.vector.tensor_tensor(keep[:, J:CE], d[:, J:CE], d[:, 0:CE - J], ALU.is_equal)
                nc.vector.memset(end[:, CE - J:CE], 1.0)
                nc.vector.tensor_tensor(end[:, 0:CE - J], d[:, J:CE], d[:, 0:CE - J],
                                        ALU.not_equal).then_inc(S["arrays_done"], 1)

            def open_chunk(s, slot, count=1):
                if known(s):
                    from_ = src_cols[:, J * s:J * s + J * count]
                else:
                    from_ = src_cols[:, bass.ds(s * J, J * count)]
                nc.vector.tensor_copy(idx_ring[:, slot:slot + count, :].rearrange("p r j -> p (r j)"),
                                      from_).then_inc(S["chunk_open"], count)

            def build_onehot(s, par):
                nc.vector.tensor_tensor(onehot[:, par, :, :], iota_n[:].unsqueeze(1).broadcast_to([P, J, P]),
                                        loc_cols[:, bass.ds(s * J, J)].unsqueeze(2).broadcast_to([P, J, P]),
                                        ALU.is_equal).then_inc(S["onehot_ready"], 1)

            def widen_keep(s):
                nc.vector.tensor_copy(keep_wide[:].rearrange("p (j d) -> p j d", j=J),
                                      keep_cols[:, bass.ds(s * J, J)].unsqueeze(2).broadcast_to([P, J, D])
                                      ).then_inc(S["wide_ready"], 1)

            dve.wait_ge(S["prep_out"], 1)
            open_chunk(0, 0, RING)
            dve.wait_ge(S["prep_out"], 4 * B)
            dve.wait_ge(S["at_ready"], 1)
            build_onehot(0, 0)
            widen_keep(0)

            def mask_ends(s):
                dve.wait_ge(S["ends_turned"], s + 1)
                nc.vector.tensor_tensor(ends[:], ps_ends[:, 0:P].rearrange("p (j d) -> p j d", j=J),
                                        end_cols[:, bass.ds(s * J, J)].unsqueeze(2).broadcast_to([P, J, D]),
                                        ALU.mult).then_inc(S["ends_ready"], 1)

            def keep_best(s):
                at = dve.value_load(best_at[0:1, bass.ds(s, 1)], min_val=0, max_val=(NW - 1) * D)
                dve.wait_ge(S["pick_ready"], s + 1)
                nc.vector.tensor_reduce(picked4[:], ps_pick[:, 0:P].rearrange("p (j d) -> p d j", j=J),
                                        AX.X, ALU.max).then_inc(S["picked_max"], 1)
                dve.wait_ge(S["picked_max"], s + 1)
                if known(s) and s == 0:
                    dve.wait_ge(S["best_zero"], 1)
                else:
                    dve.wait_ge(S["best_done"], s)
                col = flat_best[:, bass.ds(at, D)]
                nc.vector.tensor_tensor(col, col, picked4[:], ALU.max).then_inc(S["best_done"], 1)

            def step(s, slot, turn):
                dve.wait_ge(S["feat_turned"], s + 1)
                open_chunk(s + RING, slot)
                if not (known(s) and s == 0):
                    mask_ends(s - 1)
                    keep_best(s - 1)
                build_onehot(s + 1, (slot + 1) % 2)
                dve.wait_ge(S["val_ready"], s + 1)
                dve.wait_ge(S["keep_ready"], s + 1)
                nc.vector.tensor_tensor_scan(running[:], ps_keep[:, 0:P], value[:], 0.0, ALU.mult,
                                             ALU.max).then_inc(S["run_ready"], 1)
                widen_keep(s + 1)

            steps(dve, step)
            mask_ends(C - 1)
            keep_best(C - 1)

            even = best[:].rearrange("p (t o) d -> p t o d", o=2)[:, :, 0, :]
            nc.vector.memset(shifted[0:P // 2, 0, :], 0.0).then_inc(S["shift_pad"], 1)
            dve.wait_ge(S["best_done"], C)
            nc.vector.tensor_tensor(even, even, h_win[:, 0:T, :], ALU.max).then_inc(S["final_step"], 1)
            dve.wait_ge(S["odd_out"], 32)
            dve.wait_ge(S["final_step"], 1)
            dve.wait_ge(S["shift_pad"], 1)
            nc.vector.tensor_tensor(even, even, shifted, ALU.max).then_inc(S["final_step"], 1)
            dve.wait_ge(S["final_step"], 2)
            dve.wait_ge(S["x_win_in"], 32)
            nc.vector.tensor_tensor(x_even[:], x_even[:], even, ALU.add).then_inc(S["out_ready"], 1)


_OUT = "out_dram"


def kernel(x, src, dst, edge_attr_32, L0_gnn_W1, L0_gnn_b1, L0_gnn_W2, L0_gnn_b2):
    import numpy as np
    import concourse.bacc as bacc
    from concourse.bass_utils import run_bass_kernel_spmd

    nc = bacc.Bacc("TRN2", target_bir_lowering=False, num_devices=1)
    given = dict(x=x, src=src, dst=dst, edge_attr=edge_attr_32, W1=L0_gnn_W1, b1=L0_gnn_b1, W2=L0_gnn_W2,
                 b2=L0_gnn_b2)
    arrays, aps = {}, {}
    for name, a in given.items():
        a = np.ascontiguousarray(a)
        arrays[name + "_in"] = a
        aps[name] = nc.dram_tensor(name + "_in", a.shape, mybir.dt.from_np(a.dtype), kind="ExternalInput").ap()
    aps["out"] = nc.dram_tensor(_OUT, arrays["x_in"].shape, F32, kind="ExternalOutput").ap()
    gnn_layer(nc, **aps)
    r = run_bass_kernel_spmd(nc, [arrays], core_ids=[0])
    return r.results[0][_OUT]
```

```python
from contextlib import ExitStack

import concourse.bass as bass
from concourse import mybir

F32 = mybir.dt.float32
BF16 = mybir.dt.bfloat16
I32 = mybir.dt.int32
U32 = mybir.dt.uint32
ALU = mybir.AluOpType
ACT = mybir.ActivationFunctionType
AX = mybir.AxisListType

P = 128
J = 4
CE = P * J
RING = 6
HOT = 3
OUT_PART = 12
EPS = 1e-5


def gnn_layer(nc, x, src, dst, edge_attr, W1, b1, W2, b2, out):
    N, D = x.shape
    E = src.shape[0]
    HID = W1.shape[1]
    C = -(-E // CE)
    LAST = E - CE
    T = -(-N // P)
    NW = 2 * T
    TAIL = N - (T - 1) * P
    TG = -(-(T + 1) // J)
    B = -(-C // P)
    assert D == 32 and HID == 64 and W2.shape[1] == D and C > 2 and (C - 2) % RING == RING % HOT == 0
    FULLP = N // T
    REST = N - FULLP * T
    assert FULLP < P

    h_dram = nc.dram_tensor("h_rows", (N, D), F32, kind="Internal").ap()

    def chunks_of(b):
        return min(P, C - b * P)

    ctx = ExitStack()
    with ctx:
        def sb(name, shape, dt=F32):
            return ctx.enter_context(nc.sbuf_tensor(name, shape, dt))

        def pb(name, shape, dt=F32):
            return ctx.enter_context(nc.psum_tensor(name, shape, dt))

        def sem(name):
            return ctx.enter_context(nc.semaphore(name))

        node_term = sb("node_term", [P, 2 * J * TG, HID])
        best = sb("best", [P, NW, D])
        h_win = sb("h_win", [P, J * TG, D])
        x_even = sb("x_even", [P, T, D])
        dst_rows = sb("dst_rows", [P, B, CE], I32)
        src_cols = sb("src_cols", [P, J * (C + RING)], I32)
        loc_cols = sb("loc_cols", [P, J * (C + 1)])
        end_cols = sb("end_cols", [P, J * C])
        keep_cols = sb("keep_cols", [P, J * (C + 1)], BF16)
        firsts = sb("firsts", [1, C + 1], I32)
        best_at = sb("best_at", [1, C + 1], I32)
        term_at = sb("term_at", [1, C + 1], I32)
        ident = sb("ident", [P, P])
        ident_bf = sb("ident_bf", [P, P], BF16)
        iota_n = sb("iota_n", [P, P])
        iota_i = sb("iota_i", [P, P], I32)
        w1_pair = sb("w1_pair", [P, P])
        w1_dst = sb("w1_dst", [P, J, HID])
        w2_pair = sb("w2_pair", [P, 2 * D])
        b1_col = sb("b1_col", [P, 1])
        b2_col = sb("b2_col", [P, 1])
        idx_ring = sb("idx_ring", [P, RING, J], I32)
        feat = sb("feat", [P, RING, 2, 2, 2 * D])
        onehot = sb("onehot", [P, HOT, J, P])
        onehot_t = sb("onehot_t", [P, J, P])
        keep_wide = sb("keep_wide", [P, P], BF16)
        term = sb("term", [P, HID])
        feat_t = sb("feat_t", [P, 2, P])
        hidden = sb("hidden", [P, 2, P])
        value = sb("value", [P, P])
        running = sb("running", [P, P])
        ends = sb("ends", [P, J, D])
        picked4 = sb("picked4", [P, D])
        wrong = sb("wrong", [P, B + 2])
        places = sb("places", [P, 2, B])
        worst = sb("worst", [P, 1])
        flag_f = sb("flag_f", [1, 1])
        flag = sb("flag", [1, 1], I32)
        any_idx = sb("any_idx", [P, 2, J], I32)
        mean = sb("mean", [P, T])
        var = sb("var", [P, T])
        rstd = sb("rstd", [P, T])
        base_i = sb("base_i", [P, B], I32)
        base_f = sb("base_f", [P, B])
        prep = sb("prep", [P, 2, 4, CE])
        root_first = sb("root_first", [P, 1])

        flat_term = node_term[:].rearrange("p w k -> p (w k)")
        cent = flat_term[:, 0:T * D].rearrange("p (t d) -> p t d", d=D)
        sq = flat_term[:, T * D:2 * T * D].rearrange("p (t d) -> p t d", d=D)
        h_even = sq
        src_rows = flat_term[:, 2 * T * D:2 * T * D + B * CE].bitcast(I32).rearrange("p (b e) -> p b e", e=CE)
        assert 2 * T * D + B * CE <= 2 * J * TG * HID

        ps_feat_bank = pb("ps_feat_bank", [P, 4 * P])
        ps_feat = ps_feat_bank[:, 0:2 * P].rearrange("p (c q) -> p c q", c=2)
        ps_onehot = pb("ps_onehot", [P, J, P])
        ps_hidden = pb("ps_hidden", [P, 2, 2 * P])
        ps_value = pb("ps_value", [P, 4 * P])
        ps_keep = pb("ps_keep", [P, 4 * P])
        ps_ends = pb("ps_ends", [P, 4 * P])
        ps_pick = pb("ps_pick", [P, 4 * P])
        ps_flag = pb("ps_flag", [P, 4 * P])

        rows_bank = (ps_feat_bank[:], ps_onehot[:].rearrange("p j q -> p (j q)"), ps_ends[:], ps_pick[:])
        src_bank = (rows_bank[0], rows_bank[3])
        term_bank = (ps_keep[:, 0:J * HID], ps_hidden[:, 1, 0:J * HID], rows_bank[1][:, 0:J * HID],
                     rows_bank[2][:, 0:J * HID])
        turned_h = (hidden, feat_t)
        HALF = P // 2

        PIECES = [(0, FULLP // 16 * 16), (FULLP // 16 * 16, FULLP)]

        s_names = """const_ready root_ready w_zero w_in row_pad pads best_zero src_in dst_in firsts_in best_in x_win_in
            cent_done sq_done var_ready std_ready norm_step h_even_done h_stored
            src_cast src_turned src_cols_out at_ready base_step fall_done arrays_done dst_turned dst_cols_out """
        s_names += """chunk_open chunk_begun feat_turned feat_t_ready onehot_ready onehot_turned onehot_t_ready
            term_ready hid_sum hid_ready val_sum val_ready wide_ready keep_ready run_ready ends_turned
            ends_ready pick_ready picked_max best_done """
        s_names += """check_step worst_ready flag_turned flag_ready
            shifted shift_pad both_halves out_ready out_done
            any_in any_gather_begun any_gathered any_turned any_t_ready any_hid_sum any_hid_ready
            any_val_sum any_val_ready any_zero any_begun any_done
            any_copied any_block_turned any_block_max any_block_done"""
        S = {n: sem(n) for n in s_names.split()}
        s_gather = [sem(f"gathered{r}") for r in range(RING)]
        s_attr = [sem(f"attr_in{r}") for r in range(RING)]
        s_x = [sem(f"x_in{n}") for n in range(2)]
        s_hwin = [sem(f"h_win_in{n}") for n in range(4)]

        s_ht_turned, s_ht_out, s_term_made, s_term_out = (
            [sem(f"{n}{par}") for par in range(2)] for n in ("ht_turned", "ht_out", "term_made", "term_out"))

        halves = [(0, T // 2), (T // 2, T)]
        NP = FULLP + 1
        part = J * -(-TG // 4)
        h_parts = [(a, min(a + part, T)) for a in range(0, T, part)]
        out_parts = [(a, min(a + OUT_PART, T)) for a in range(0, T, OUT_PART)]
        assert out_parts[-1][1] - out_parts[-1][0] > 1
        PER_HALF = [16 * (sum(z > a for a, z in PIECES) + (REST > t0)) for t0, _ in halves]
        EVEN = sum(PER_HALF)

        even_best, odd_best = (best[:].rearrange("p (t o) d -> p t o d", o=2)[:, :, o, :] for o in range(2))
        flat_best = best[:].rearrange("p w d -> p (w d)")
        flat_h = h_win[:].rearrange("p t d -> p (t d)")
        any_dst = prep[0:1, 0, 0, :].bitcast(I32)
        any_best = flat_term[:, 0:T * P]
        shifted = flat_term[:, 0:T * D].rearrange("p (t d) -> p t d", d=D)

        def steps(eng, step, after={}):
            for s in range(2):
                step(s, s % RING, s // RING)
                if s in after:
                    after[s]()
            with eng.Fori(0, (C - 2) // RING) as i:
                for u in range(RING):
                    step(i * RING + (2 + u), (2 + u) % RING, i + (2 + u) // RING)

        def any_steps(eng, any_step):
            with eng.Fori(0, C - 1) as c:
                any_step(c, c * CE)
            any_step(C - 1, LAST)

        def known(s):
            return isinstance(s, int)

        def even_dmas(dma, dram, tile, to_dram, t0, t1, done):
            n = 0
            for a, z in PIECES:
                if z > a:
                    d = dram[a * T:z * T, :].rearrange("(p t) d -> p t d", t=T)[:, t0:t1, :]
                    s_ = tile[a:z, t0:t1, :]
                    (dma(d, s_) if to_dram else dma(s_, d)).then_inc(done, 16)
                    n += 16
            t1 = min(t1, REST)
            if t1 > t0:
                d = dram[FULLP * T + t0:FULLP * T + t1, :].rearrange("(p t) d -> p t d", p=1)
                s_ = tile[FULLP:FULLP + 1, t0:t1, :]
                (dma(d, s_) if to_dram else dma(s_, d)).then_inc(done, 16)
                n += 16
            return n

        def win_dmas(dma, dram, tile, to_dram, t0, t1, done):
            full = min(t1, T - 1)
            d = dram[t0 * P:full * P, :].rearrange("(t p) d -> p t d", p=P)
            s_ = tile[:, t0:full, :]
            (dma(d, s_) if to_dram else dma(s_, d)).then_inc(done, 16)
            if t1 == T:
                d = dram[(T - 1) * P:N, :]
                s_ = tile[0:TAIL, T - 1, :]
                (dma(d, s_) if to_dram else dma(s_, d)).then_inc(done, 16)

        def row_dmas(dma, vec, tile, done):
            for b in range(B):
                whole = min(P, C - 1 - b * P)
                dma(tile[0:whole, b, :],
                    vec[b * P * CE:(b * P + whole) * CE].rearrange("(q e) -> q e", e=CE)).then_inc(done, 16)
                if b == B - 1:
                    dma(tile[whole:whole + 1, b, :],
                        vec[LAST:E].rearrange("(q e) -> q e", q=1)).then_inc(done, 16)

        NROW = B + 1
        attr = edge_attr.rearrange("e f -> (e f)")
        NBD = 4 + 2 + J + 2 + J

        def node_terms(eng, copy, par):
            groups = list(range(par, TG, 2))

            def take_turned(n):
                eng.wait_ge(s_ht_turned[par], n + 1)
                if n >= 2:
                    eng.wait_ge(s_term_made[par], n - 1)
                copy(turned_h[par][:, n % 2, :], (ps_value, ps_flag)[par][:, 0:P]).then_inc(s_ht_out[par], 1)

            take_turned(0)
            for n, g in enumerate(groups):
                if n + 1 < len(groups):
                    take_turned(n + 1)
                eng.wait_ge(s_term_made[par], n + 1)
                made = term_bank[g % 4].rearrange("p (t k) -> p t k", t=J)
                w = 2 * J * g
                copy(node_term[:, w:w + 2 * J:2, :], made)
                copy(node_term[0:HALF, w + 1:w + 2 * J:2, :], made[HALF:P, :, :])
                t0 = 1 if g == 0 else 0
                copy(node_term[HALF:P, w + 2 * t0 - 1:w + 2 * J - 1:2, :],
                     made[0:HALF, t0:J, :]).then_inc(s_term_out[par], 1)

        block = ctx.enter_context(nc.Block())

        @block.sync
        def _(sp):
            for n, (a, z) in enumerate(halves):
                even_dmas(sp.dma_start, x, x_even, False, a, z, s_x[n])
            sp.dma_start(x_even[FULLP:FULLP + 1, REST:T, :],
                         x[0:T - REST, :].rearrange("(p t) d -> p t d", p=1)).then_inc(s_x[1], 16)
            row_dmas(sp.dma_start, src, src_rows, S["src_in"])
            sp.wait_ge(S["row_pad"], 2)
            row_dmas(sp.dma_start, dst, dst_rows, S["dst_in"])
            sp.dma_start(firsts[:, 0:C - 1],
                         dst[0:(C - 1) * CE].rearrange("(a c e) -> a c e", a=1, e=CE)[:, :, 0],
                         allow_slow_non_contiguous=True).then_inc(S["firsts_in"], 16)
            sp.dma_start(firsts[:, C - 1:C],
                         dst[LAST:LAST + 1].rearrange("(a c) -> a c", a=1)).then_inc(S["firsts_in"], 16)
            for n, (a, z) in enumerate(halves):
                sp.wait_ge(S["h_even_done"], n + 1)
                even_dmas(sp.dma_start, h_dram, h_even, True, a, z, S["h_stored"])
            sp.wait_ge(S["h_stored"], EVEN)
            sp.wait_ge(S["pads"], 4)
            for n, (a, z) in enumerate(h_parts):
                win_dmas(sp.dma_start, h_dram, h_win, False, a, z, s_hwin[n])

            def step(s, slot, turn):
                sp.wait_ge(S["chunk_open"], s + 1)
                sp.dma_start(feat[:, slot, :, 1, :],
                             attr[bass.ds(s * (CE * D), CE * D)].rearrange("(p c k) -> p c k", p=P, c=2)
                             ).then_inc(s_attr[slot], 16)

            for s in range(RING):
                step(s, s % RING, 0)
            sp.wait_ge(S["best_zero"], 1)
            win_dmas(sp.dma_start, h_dram, even_best, False, 0, T, S["best_in"])
            win_dmas(sp.dma_start, x, x_even, False, 0, T, S["x_win_in"])
            turns = (C - 1 - RING) // RING
            with sp.Fori(0, turns) as i:
                for u in range(RING):
                    step(i * RING + (RING + u), u, 0)
            for s in range(RING + RING * turns, C - 1):
                step(s, s % RING, 0)
            sp.wait_ge(S["chunk_open"], C)
            sp.dma_start(feat[:, (C - 1) % RING, :, 1, :],
                         attr[LAST * D:E * D].rearrange("(p c k) -> p c k", p=P, c=2)).then_inc(s_attr[(C - 1) % RING], 16)

            sp.wait_ge(S["best_done"], C)
            sp.wait_ge(S["flag_ready"], 1)
            with sp.If(sp.value_load(flag[0:1, 0:1], min_val=0, max_val=1)):
                def any_step(c, base):
                    sp.wait_ge(S["any_done"], c + 1)
                    sp.dma_start(feat[:, 0, :, 1, :],
                                 attr[bass.ds(base * D, CE * D)].rearrange("(p c k) -> p c k", p=P, c=2)
                                 ).then_inc(S["any_in"], 16)
                    for n, vec in enumerate((src, dst)):
                        sp.dma_start(any_idx[:, n, :], vec[bass.ds(base, CE)].rearrange("(p j) -> p j", j=J)
                                     ).then_inc(S["any_in"], 16)
                    sp.dma_start(any_dst, dst[bass.ds(base, CE)].rearrange("(a e) -> a e", a=1)
                                 ).then_inc(S["any_in"], 16)

                any_steps(sp, any_step)
            for n, (a, z) in enumerate(out_parts):
                sp.wait_ge(S["out_ready"], n + 1 + (z == T))
                win_dmas(sp.dma_start, out, x_even, True, a, z, S["out_done"])
            sp.wait_ge(S["out_done"], 16 * len(out_parts) + 16)

        @block.gpsimd
        def _(pool):
            nc.gpsimd.memset(ident[:], 0.0).then_inc(S["const_ready"], 1)
            pool.wait_ge(S["const_ready"], 1)
            nc.gpsimd.affine_select(out=ident[:], in_=ident[:], compare_op=ALU.not_equal, fill=1.0, base=0,
                                    pattern=[[-1, P]], channel_multiplier=1).then_inc(S["const_ready"], 1)
            nc.gpsimd.iota(iota_i[:], pattern=[[1, P]], base=0, channel_multiplier=0).then_inc(S["const_ready"], 1)
            pool.wait_ge(S["w_zero"], 3)
            for z, row in enumerate((0, 2 * D)):
                for a in range(2):
                    k = 2 * D * z + D * a
                    pool.dma_start(w1_pair[k:k + D, HID * a:HID * a + HID], W1[row:row + D, :]).then_inc(S["w_in"], 16)
            for t in range(J):
                pool.dma_start(w1_dst[D * t:D * t + D, t, :], W1[D:2 * D, :]).then_inc(S["w_in"], 16)
                pool.dma_start(b2_col[D * t:D * t + D, :], b2.rearrange("(p a) -> p a", a=1)).then_inc(S["w_in"], 16)
            for a in range(2):
                pool.dma_start(w2_pair[HID * a:HID * a + HID, D * a:D * a + D], W2).then_inc(S["w_in"], 16)
                pool.dma_start(b1_col[HID * a:HID * a + HID, :], b1.rearrange("(p a) -> p a", a=1)).then_inc(S["w_in"], 16)
            nc.gpsimd.memset(best[:], 0.0).then_inc(S["best_zero"], 1)
            pool.wait_ge(S["h_stored"], EVEN)

            def step(s, slot, turn):
                pool.wait_ge(S["chunk_open"], s + 1)
                pool.sem_inc(S["chunk_begun"], 1)
                for j in range(J):
                    nc.gpsimd.indirect_dma_start(
                        feat[:, slot, j // 2, 0, D * (j % 2):D * (j % 2) + D], None, h_dram,
                        bass.IndirectOffsetOnAxis(ap=idx_ring[:, slot, j:j + 1].bitcast(U32), axis=0),
                    ).then_inc(s_gather[slot], 16)

            steps(pool, step)

            pool.wait_ge(S["flag_ready"], 1)
            with pool.If(pool.value_load(flag[0:1, 0:1], min_val=0, max_val=1)):
                def any_step(c, base):
                    pool.wait_ge(S["any_in"], c * 64 + 64)
                    pool.sem_inc(S["any_gather_begun"], 1)
                    for j in range(J):
                        for n, to in enumerate((feat[:, 0, j // 2, 0, D * (j % 2):D * (j % 2) + D], ends[:, j, :])):
                            nc.gpsimd.indirect_dma_start(
                                to, None, h_dram,
                                bass.IndirectOffsetOnAxis(ap=any_idx[:, n, j:j + 1].bitcast(U32), axis=0),
                            ).then_inc(S["any_gathered"], 16)

                any_steps(pool, any_step)

        @block.tensor
        def _(pe):
            pe.wait_ge(S["const_ready"], 5)

            def turn_rows(b, a, done, bank):
                q = chunks_of(b)
                for j in range(J):
                    mm = pe.transpose(bank[:, P * j:P * j + q], prep[0:q, b % 2, a, j:CE:J],
                                      ident[0:q, 0:q])
                mm.then_inc(done, 1)

            for b in range(B):
                pe.wait_ge(S["src_cast"], b + 1)
                if b >= 2:
                    pe.wait_ge(S["src_cols_out"], b - 1)
                turn_rows(b, 0, S["src_turned"], src_bank[b % 2])
            pe.wait_ge(S["src_cols_out"], B)
            for b in range(B):
                pe.wait_ge(S["arrays_done"], b + 1)
                for a in range(1, 4):
                    if b >= 1:
                        pe.wait_ge(S["dst_cols_out"], 3 * (b - 1) + a)
                    turn_rows(b, a, S["dst_turned"], rows_bank[a])
            pe.wait_ge(S["w_in"], 16 * NBD)

            def turn_h(g):
                for n, (a, z) in enumerate(h_parts):
                    if a == J * g:
                        pe.wait_ge(s_hwin[n], 32 if z == T else 16)
                if g >= 2:
                    pe.wait_ge(s_ht_out[g % 2], g // 2)
                pe.transpose((ps_value, ps_flag)[g % 2][:, 0:P],
                             h_win[:, J * g:J * g + J, :].rearrange("p t d -> p (t d)"),
                             ident[:]).then_inc(s_ht_turned[g % 2], 1)

            for g in range(3):
                turn_h(g)
            for g in range(TG):
                if g + 3 < TG:
                    turn_h(g + 3)
                pe.wait_ge(s_ht_out[g % 2], g // 2 + 1)
                if g == 2:
                    pe.wait_ge(S["dst_cols_out"], 3 * B)
                if g >= 4:
                    pe.wait_ge(s_term_out[g % 2], g // 2 - 1)
                pe.matmul(term_bank[g % 4], turned_h[g % 2][:, g // 2 % 2, :], w1_dst[:].rearrange("p t k -> p (t k)"),
                          start=True, stop=True).then_inc(s_term_made[g % 2], 1)
            for par in range(2):
                pe.wait_ge(s_term_out[par], (TG + 1 - par) // 2)
            pe.wait_ge(S["dst_cols_out"], 3 * B)

            def pick(s, slot):
                pe.wait_ge(S["ends_ready"], s + 1)
                for j in range(J):
                    mm = pe.matmul(ps_pick[:, D * j:D * j + D], onehot[:, slot, j, :], ends[:, j, :],
                                   start=(j == 0), stop=(j == J - 1), skip_group_check=True)
                mm.then_inc(S["pick_ready"], 1)

            def turn_best(s):
                pe.wait_ge(S["run_ready"], s + 1)
                pe.transpose(ps_ends[:, 0:P], running[:], ident[:]).then_inc(S["ends_turned"], 1)

            def step(s, slot, turn):
                pe.wait_ge(s_gather[slot], (turn + 1) * (16 * J))
                pe.wait_ge(s_attr[slot], (turn + 1) * 16)
                for c in range(2):
                    mm = pe.transpose(ps_feat[:, c, :], feat[:, slot, c, :, :].rearrange("p z k -> p (z k)"), ident[:])
                mm.then_inc(S["feat_turned"], 1)
                pe.wait_ge(S["onehot_ready"], s + 1)
                for j in range(J):
                    mm = pe.transpose(ps_onehot[:, j, :], onehot[:, slot % HOT, j, :], ident[:])
                mm.then_inc(S["onehot_turned"], 1)
                if not (known(s) and s == 0):
                    turn_best(s - 1)
                pe.wait_ge(S["wide_ready"], s + 1)
                pe.matmul(ps_keep[:, 0:P], keep_wide[:], ident_bf[:], start=True,
                          stop=True).then_inc(S["keep_ready"], 1)
                pe.wait_ge(S["feat_t_ready"], s + 1)
                for c in range(2):
                    pe.matmul(ps_hidden[:, 0, P * c:P * c + P], w1_pair[:], feat_t[:, c, :],
                              start=(c == 0), stop=False, skip_group_check=True)
                pe.wait_ge(S["term_ready"], s + 1)
                pe.wait_ge(S["onehot_t_ready"], s + 1)
                for a in range(2):
                    mm = pe.matmul(ps_hidden[HID * a:HID * a + HID, 0, :], term[:], onehot_t[:, a:J:2, :],
                                   start=False, stop=True, skip_group_check=True)
                mm.then_inc(S["hid_sum"], 1)
                if not (known(s) and s == 0):
                    pick(s - 1, (slot - 1) % HOT)
                pe.wait_ge(S["hid_ready"], s + 1)
                for c in range(2):
                    mm = pe.matmul(ps_value[HID * c:HID * c + HID, 0:P], w2_pair[:], hidden[:, c, :],
                                   start=True, stop=True, skip_group_check=True)
                mm.then_inc(S["val_sum"], 1)

            def turn_worst():
                pe.wait_ge(S["worst_ready"], 1)
                pe.transpose(ps_flag[0:1, 0:P], worst[:], ident[:]).then_inc(S["flag_turned"], 1)

            steps(pe, step, {1: turn_worst})
            turn_best(C - 1)
            pick(C - 1, (C - 1) % HOT)

            pe.wait_ge(S["flag_ready"], 1)
            with pe.If(pe.value_load(flag[0:1, 0:1], min_val=0, max_val=1)):
                def any_step(c, base):
                    pe.wait_ge(S["any_gathered"], c * (32 * J) + 32 * J)
                    for k in range(2):
                        pe.transpose(ps_feat[:, k, :], feat[:, 0, k, :, :].rearrange("p z k -> p (z k)"), ident[:])
                    pe.transpose(ps_onehot[:, 0, :], ends[:].rearrange("p j d -> p (j d)"),
                                 ident[:]).then_inc(S["any_turned"], 1)
                    pe.wait_ge(S["any_t_ready"], c * 2 + 2)
                    for k in range(2):
                        pe.matmul(ps_hidden[:, 0, P * k:P * k + P], w1_pair[:], feat_t[:, k, :], start=(k == 0),
                                  stop=False, skip_group_check=True)
                    for k in range(2):
                        mm = pe.matmul(ps_hidden[:, 0, P * k:P * k + P],
                                       w1_dst[:, 2 * k:2 * k + 2, :].rearrange("p t k -> p (t k)"),
                                       onehot_t[:, 0, :], start=False, stop=True, skip_group_check=True)
                    mm.then_inc(S["any_hid_sum"], 1)
                    pe.wait_ge(S["any_hid_ready"], c + 1)
                    for k in range(2):
                        mm = pe.matmul(ps_value[HID * k:HID * k + HID, 0:P], w2_pair[:], hidden[:, k, :],
                                       start=True, stop=True, skip_group_check=True)
                    mm.then_inc(S["any_val_sum"], 1)

                any_steps(pe, any_step)
                with pe.Fori(0, T) as t:
                    pe.wait_ge(S["any_copied"], t + 1)
                    pe.transpose(ps_ends[:, 0:P], running[:], ident[:]).then_inc(S["any_block_turned"], 1)

        @block.scalar
        def _(act):
            act.wait_ge(S["root_ready"], 1)
            nc.scalar.activation(root_first[:], root_first[:], ACT.Sqrt)
            for n, (a, z) in enumerate(halves):
                act.wait_ge(S["cent_done"], n + 1)
                nc.scalar.activation(sq[0:NP, a:z, :], cent[0:NP, a:z, :], ACT.Square).then_inc(S["sq_done"], 1)
            act.wait_ge(S["var_ready"], 1)
            nc.scalar.activation(mean[0:NP, :], var[0:NP, :], ACT.Sqrt).then_inc(S["std_ready"], 1)

            act.wait_ge(S["src_in"], 16 * NROW)

            def cast(b):
                q = chunks_of(b)
                if b >= 2:
                    act.wait_ge(S["src_turned"], b - 1)
                nc.scalar.copy(prep[0:q, b % 2, 0, :], src_rows[0:q, b, :]).then_inc(S["src_cast"], 1)

            def columns(b, bank, table, done):
                q = chunks_of(b)
                to = table[:, J * P * b:J * P * b + J * q].rearrange("p (q j) -> p j q", j=J)
                nc.scalar.copy(to, bank.rearrange("p (j q) -> p j q", j=J)[:, :, 0:q]).then_inc(done, 1)

            cast(0)
            for b in range(B):
                if b + 1 < B:
                    cast(b + 1)
                act.wait_ge(S["src_turned"], b + 1)
                columns(b, src_bank[b % 2], src_cols, S["src_cols_out"])
            for b in range(B):
                for a, table in enumerate((loc_cols, keep_cols, end_cols)):
                    act.wait_ge(S["dst_turned"], 3 * b + a + 1)
                    columns(b, rows_bank[a + 1], table, S["dst_cols_out"])

            node_terms(act, nc.scalar.copy, 0)
            act.wait_ge(s_term_out[0], (TG + 1) // 2)
            act.wait_ge(s_term_out[1], TG // 2)
            act.wait_ge(S["at_ready"], 2)

            def step(s, slot, turn):
                at = act.value_load(term_at[0:1, bass.ds(s, 1)], min_val=0, max_val=(NW - 1) * HID)
                nc.scalar.copy(term[:], flat_term[:, bass.ds(at, HID)]).then_inc(S["term_ready"], 1)
                act.wait_ge(S["feat_turned"], s + 1)
                nc.scalar.copy(feat_t[:], ps_feat).then_inc(S["feat_t_ready"], 1)
                act.wait_ge(S["onehot_turned"], s + 1)
                nc.scalar.copy(onehot_t[:], ps_onehot[:]).then_inc(S["onehot_t_ready"], 1)
                act.wait_ge(S["hid_sum"], s + 1)
                nc.scalar.activation(hidden[:], ps_hidden[:, 0, :].rearrange("p (c q) -> p c q", c=2), ACT.Relu,
                                     bias=b1_col[:, 0:1]).then_inc(S["hid_ready"], 1)
                act.wait_ge(S["val_sum"], s + 1)
                nc.scalar.activation(value[:], ps_value[:, 0:P], ACT.Identity,
                                     bias=b2_col[:, 0:1]).then_inc(S["val_ready"], 1)

            act.wait_ge(S["w_in"], 16 * NBD)
            steps(act, step)

            act.wait_ge(S["flag_ready"], 1)
            with act.If(act.value_load(flag[0:1, 0:1], min_val=0, max_val=1)):
                def any_step(c, base):
                    act.wait_ge(S["any_turned"], c + 1)
                    nc.scalar.copy(feat_t[:], ps_feat).then_inc(S["any_t_ready"], 1)
                    nc.scalar.copy(onehot_t[:, 0, :], ps_onehot[:, 0, :]).then_inc(S["any_t_ready"], 1)
                    act.wait_ge(S["any_hid_sum"], c + 1)
                    nc.scalar.activation(hidden[:], ps_hidden[:, 0, :].rearrange("p (c q) -> p c q", c=2), ACT.Relu,
                                         bias=b1_col[:, 0:1]).then_inc(S["any_hid_ready"], 1)
                    act.wait_ge(S["any_val_sum"], c + 1)
                    nc.scalar.activation(value[:], ps_value[:, 0:P], ACT.Identity,
                                         bias=b2_col[:, 0:1]).then_inc(S["any_val_ready"], 1)

                any_steps(act, any_step)
                act.wait_ge(S["any_block_done"], T + 1)

            act.wait_ge(S["best_done"], C)
            for a, z in out_parts:
                nc.scalar.copy(shifted[HALF:P, a:z, :], odd_best[0:HALF, a:z, :]).then_inc(S["shifted"], 1)
                a = max(a, 1)
                nc.scalar.copy(shifted[0:HALF, a:z, :], odd_best[HALF:P, a - 1:z - 1, :]).then_inc(S["shifted"], 1)

        @block.vector
        def _(dve):
            nc.vector.memset(root_first[:], 1.0).then_inc(S["root_ready"], 1)
            for tile in (w1_pair, w1_dst, w2_pair):
                nc.vector.memset(tile[:], 0.0).then_inc(S["w_zero"], 1)
            nc.vector.memset(dst_rows[:, B - 1, :], 0).then_inc(S["row_pad"], 1)
            nc.vector.memset(wrong[:], 0.0)
            nc.vector.memset(firsts[:, C:C + 1], 0).then_inc(S["row_pad"], 1)
            nc.vector.memset(h_win[:, T - 1:J * TG, :], 0.0).then_inc(S["pads"], 1)
            nc.vector.memset(src_cols[:, J * C:J * (C + RING)], 0).then_inc(S["pads"], 1)
            nc.vector.memset(loc_cols[:, J * C:J * (C + 1)], 0.0).then_inc(S["pads"], 1)
            nc.vector.memset(keep_cols[:, J * C:J * (C + 1)], 0.0).then_inc(S["pads"], 1)
            n = 0
            for i, (a, z) in enumerate(halves):
                dve.wait_ge(s_x[i], PER_HALF[i] + 16 * i)
                nc.vector.reduce_sum(mean[0:NP, a:z], x_even[0:NP, a:z, :], AX.X).then_inc(S["norm_step"], 1)
                dve.wait_ge(S["norm_step"], n + 1)
                nc.vector.tensor_scalar(mean[0:NP, a:z], mean[0:NP, a:z], 1.0 / D, None,
                                        ALU.mult).then_inc(S["norm_step"], 1)
                dve.wait_ge(S["norm_step"], n + 2)
                nc.vector.tensor_tensor(cent[0:NP, a:z, :], x_even[0:NP, a:z, :],
                                        mean[0:NP, a:z].unsqueeze(2).broadcast_to([NP, z - a, D]),
                                        ALU.subtract).then_inc(S["cent_done"], 1)
                n += 2
            for i, (a, z) in enumerate(halves):
                dve.wait_ge(S["sq_done"], i + 1)
                nc.vector.reduce_sum(var[0:NP, a:z], sq[0:NP, a:z, :], AX.X).then_inc(S["norm_step"], 1)
                n += 1
            dve.wait_ge(S["norm_step"], n)
            nc.vector.tensor_scalar(var[0:NP, :], var[0:NP, :], 1.0 / D, EPS, ALU.mult,
                                    ALU.add).then_inc(S["var_ready"], 1)
            dve.wait_ge(S["const_ready"], 3)
            nc.vector.tensor_copy(ident_bf[:], ident[:]).then_inc(S["const_ready"], 1)
            nc.vector.tensor_copy(iota_n[:], iota_i[:]).then_inc(S["const_ready"], 1)
            dve.wait_ge(S["std_ready"], 1)
            nc.vector.reciprocal(rstd[0:NP, :], mean[0:NP, :]).then_inc(S["norm_step"], 1)
            dve.wait_ge(S["norm_step"], n + 1)
            for a, z in halves:
                nc.vector.scalar_tensor_tensor(out=h_even[0:NP, a:z, :], in0=cent[0:NP, a:z, :],
                                               scalar=0.0,
                                               in1=rstd[0:NP, a:z].unsqueeze(2).broadcast_to([NP, z - a, D]),
                                               op0=ALU.max, op1=ALU.mult).then_inc(S["h_even_done"], 1)
            def open_chunk(s, slot, count=1):
                if known(s):
                    from_ = src_cols[:, J * s:J * s + J * count]
                else:
                    from_ = src_cols[:, bass.ds(s * J, J * count)]
                nc.vector.tensor_copy(idx_ring[:, slot:slot + count, :].rearrange("p r j -> p (r j)"),
                                      from_).then_inc(S["chunk_open"], count)

            dve.wait_ge(S["src_cols_out"], 1)
            open_chunk(0, 0, RING)
            dve.wait_ge(S["firsts_in"], 32)
            for table, width in ((best_at, D), (term_at, HID)):
                nc.vector.tensor_scalar(table[:], firsts[:], 6, width.bit_length() - 1, ALU.logical_shift_right,
                                        ALU.logical_shift_left).then_inc(S["at_ready"], 1)
            dve.wait_ge(S["dst_in"], 16 * NROW)
            nc.vector.tensor_scalar(base_i[:], dst_rows[:, :, 0], 6, 6, ALU.logical_shift_right,
                                    ALU.logical_shift_left).then_inc(S["base_step"], 1)
            dve.wait_ge(S["base_step"], 1)
            nc.vector.tensor_copy(base_f[:], base_i[:]).then_inc(S["base_step"], 1)
            dve.wait_ge(S["base_step"], 2)
            for b in range(B):
                q = chunks_of(b)
                if b >= 2:
                    dve.wait_ge(S["dst_turned"], 3 * (b - 1))
                d = dst_rows[0:q, b, :]
                _, loc, keep, end = (prep[0:q, b % 2, a, :] for a in range(4))
                fall = keep[:, J:CE]
                nc.vector.tensor_tensor_reduce(out=fall, in0=d[:, 0:CE - J], in1=d[:, J:CE], scale=1.0,
                                               scalar=-float(N), op0=ALU.subtract, op1=ALU.max,
                                               accum_out=wrong[0:q, b:b + 1]).then_inc(S["fall_done"], 1)
                nc.vector.memset(keep[:, 0:J], 0.0)
                nc.vector.memset(end[:, CE - J:CE], 1.0)
                nc.vector.tensor_scalar(loc, d, base_f[0:q, b:b + 1], None, ALU.subtract)
                dve.wait_ge(S["fall_done"], 2 * b + 1)
                nc.vector.tensor_scalar(end[:, 0:CE - J], fall, 0.0, None, ALU.not_equal).then_inc(S["fall_done"], 1)
                dve.wait_ge(S["fall_done"], 2 * b + 2)
                nc.vector.tensor_scalar(fall, fall, 0.0, None, ALU.is_equal).then_inc(S["arrays_done"], 1)
            nc.vector.tensor_reduce(places[:, 0, :], dst_rows[:, :, 0:J], AX.X, ALU.min).then_inc(S["check_step"], 1)
            nc.vector.tensor_reduce(places[:, 1, :], dst_rows[:, :, CE - J:CE], AX.X,
                                    ALU.max).then_inc(S["check_step"], 1)
            dve.wait_ge(S["check_step"], 2)
            nc.vector.tensor_tensor(places[:, 0, :], base_f[:], places[:, 0, :],
                                    ALU.subtract).then_inc(S["check_step"], 1)
            nc.vector.tensor_tensor(places[:, 1, :], places[:, 1, :], base_f[:],
                                    ALU.subtract).then_inc(S["check_step"], 1)
            dve.wait_ge(S["check_step"], 4)
            nc.vector.tensor_scalar(places[:, 1, :], places[:, 1, :], P - 1.0, None,
                                    ALU.subtract).then_inc(S["check_step"], 1)
            dve.wait_ge(S["check_step"], 5)
            nc.vector.tensor_reduce(wrong[:, B:B + 2], places[:], AX.X, ALU.max).then_inc(S["check_step"], 1)
            dve.wait_ge(S["check_step"], 6)
            nc.vector.tensor_reduce(worst[:], wrong[:], AX.X, ALU.max).then_inc(S["worst_ready"], 1)

            def build_onehot(s, slot):
                nc.vector.tensor_tensor(onehot[:, slot, :, :], iota_n[:].unsqueeze(1).broadcast_to([P, J, P]),
                                        loc_cols[:, bass.ds(s * J, J)].unsqueeze(2).broadcast_to([P, J, P]),
                                        ALU.is_equal).then_inc(S["onehot_ready"], 1)

            def widen_keep(s):
                nc.vector.tensor_copy(keep_wide[:].rearrange("p (j d) -> p j d", j=J),
                                      keep_cols[:, bass.ds(s * J, J)].unsqueeze(2).broadcast_to([P, J, D])
                                      ).then_inc(S["wide_ready"], 1)

            node_terms(dve, nc.vector.tensor_copy, 1)
            dve.wait_ge(S["dst_cols_out"], 3 * B)
            dve.wait_ge(S["at_ready"], 1)
            build_onehot(0, 0)
            widen_keep(0)

            def mask_ends(s):
                dve.wait_ge(S["ends_turned"], s + 1)
                nc.vector.tensor_tensor(ends[:], ps_ends[:, 0:P].rearrange("p (j d) -> p j d", j=J),
                                        end_cols[:, bass.ds(s * J, J)].unsqueeze(2).broadcast_to([P, J, D]),
                                        ALU.mult).then_inc(S["ends_ready"], 1)

            def keep_best(s):
                at = dve.value_load(best_at[0:1, bass.ds(s, 1)], min_val=0, max_val=(NW - 1) * D)
                dve.wait_ge(S["pick_ready"], s + 1)
                nc.vector.tensor_reduce(picked4[:], ps_pick[:, 0:P].rearrange("p (j d) -> p d j", j=J),
                                        AX.X, ALU.max).then_inc(S["picked_max"], 1)
                dve.wait_ge(S["picked_max"], s + 1)
                if known(s) and s == 0:
                    dve.wait_ge(S["best_in"], 32)
                else:
                    dve.wait_ge(S["best_done"], s)
                col = flat_best[:, bass.ds(at, D)]
                nc.vector.tensor_tensor(col, col, picked4[:], ALU.max).then_inc(S["best_done"], 1)

            def step(s, slot, turn):
                dve.wait_ge(S["feat_turned"], s + 1)
                open_chunk(s + RING, slot)
                build_onehot(s + 1, (slot + 1) % HOT)
                if not (known(s) and s == 0):
                    mask_ends(s - 1)
                    keep_best(s - 1)
                dve.wait_ge(S["val_ready"], s + 1)
                dve.wait_ge(S["keep_ready"], s + 1)
                nc.vector.tensor_tensor_scan(running[:], ps_keep[:, 0:P], value[:], 0.0, ALU.mult,
                                             ALU.max).then_inc(S["run_ready"], 1)
                widen_keep(s + 1)

            def check():
                dve.wait_ge(S["flag_turned"], 1)
                nc.vector.tensor_reduce(flag_f[:], ps_flag[0:1, 0:P], AX.X, ALU.max).then_inc(S["check_step"], 1)
                dve.wait_ge(S["check_step"], 7)
                nc.vector.tensor_scalar(flag[:], flag_f[:], 0.0, None, ALU.is_gt).then_inc(S["flag_ready"], 1)

            steps(dve, step, {1: check})
            mask_ends(C - 1)
            keep_best(C - 1)

            dve.wait_ge(S["best_done"], C)
            dve.wait_ge(S["flag_ready"], 1)
            with dve.If(dve.value_load(flag[0:1, 0:1], min_val=0, max_val=1)):
                nc.vector.memset(any_best, 0.0)
                nc.vector.memset(best[:], 0.0).then_inc(S["any_zero"], 1)
                dve.wait_ge(S["any_zero"], 1)
                dve.sem_inc(S["any_done"], 1)

                def any_step(c, base):
                    dve.wait_ge(S["any_in"], c * 64 + 64)
                    dve.wait_ge(S["any_val_ready"], c + 1)
                    dve.sem_inc(S["any_begun"], 1)
                    with dve.Fori(0, P) as p:
                        for j in range(J):
                            at = dve.value_load(any_dst[0:1, bass.ds(p * J + j, 1)], min_val=0, max_val=N - 1)
                            col = any_best[D * j:D * j + D, bass.ds(at, 1)]
                            nc.vector.tensor_tensor(col, col, value[D * j:D * j + D, bass.ds(p, 1)], ALU.max)
                        dve.drain()
                    dve.sem_inc(S["any_done"], 1)

                any_steps(dve, any_step)
                dve.sem_inc(S["any_block_done"], 1)
                with dve.Fori(0, T) as t:
                    dve.wait_ge(S["any_block_done"], t + 1)
                    nc.vector.tensor_copy(running[:], any_best[:, bass.ds(t * P, P)]).then_inc(S["any_copied"], 1)
                    dve.wait_ge(S["any_block_turned"], t + 1)
                    nc.vector.tensor_reduce(picked4[:], ps_ends[:, 0:P].rearrange("p (j d) -> p d j", j=J),
                                            AX.X, ALU.max).then_inc(S["any_block_max"], 1)
                    dve.wait_ge(S["any_block_max"], t + 1)
                    nc.vector.tensor_tensor(flat_best[:, bass.ds(t * (2 * D), D)], picked4[:],
                                            flat_h[:, bass.ds(t * D, D)], ALU.max).then_inc(S["any_block_done"], 1)
                dve.wait_ge(S["any_block_done"], T + 1)

            nc.vector.memset(shifted[0:HALF, 0, :], 0.0).then_inc(S["shift_pad"], 1)
            dve.wait_ge(S["shift_pad"], 1)
            dve.wait_ge(S["x_win_in"], 32)
            n = 0
            for i, (a, z) in enumerate(out_parts):
                dve.wait_ge(S["shifted"], 2 * i + 2)
                pieces = [(P, a, min(z, T - 1))] + ([(TAIL, T - 1, T)] if z == T else [])
                for rows, a, z in pieces:
                    nc.vector.tensor_tensor(even_best[0:rows, a:z, :], even_best[0:rows, a:z, :],
                                            shifted[0:rows, a:z, :], ALU.max).then_inc(S["both_halves"], 1)
                for rows, a, z in pieces:
                    n += 1
                    dve.wait_ge(S["both_halves"], n)
                    nc.vector.tensor_tensor(x_even[0:rows, a:z, :], x_even[0:rows, a:z, :],
                                            even_best[0:rows, a:z, :], ALU.add).then_inc(S["out_ready"], 1)


_OUT = "out_dram"


def kernel(x, src, dst, edge_attr_32, L0_gnn_W1, L0_gnn_b1, L0_gnn_W2, L0_gnn_b2):
    import numpy as np
    import concourse.bacc as bacc
    from concourse.bass_utils import run_bass_kernel_spmd

    nc = bacc.Bacc("TRN2", target_bir_lowering=False, num_devices=1)
    given = dict(x=x, src=src, dst=dst, edge_attr=edge_attr_32, W1=L0_gnn_W1, b1=L0_gnn_b1, W2=L0_gnn_W2,
                 b2=L0_gnn_b2)
    arrays, aps = {}, {}
    for name, a in given.items():
        a = np.ascontiguousarray(a)
        arrays[name + "_in"] = a
        aps[name] = nc.dram_tensor(name + "_in", a.shape, mybir.dt.from_np(a.dtype), kind="ExternalInput").ap()
    aps["out"] = nc.dram_tensor(_OUT, arrays["x_in"].shape, F32, kind="ExternalOutput").ap()
    gnn_layer(nc, **aps)
    r = run_bass_kernel_spmd(nc, [arrays], core_ids=[0])
    return r.results[0][_OUT]
```
